# Optimizing a Trainium2 kernel written in Bass

```python
import numpy as np
import jax
import jax.numpy as jnp

def _softmax(x, axis=-1):
    return jax.nn.softmax(x, axis=axis)

def _gelu(x):
    return jax.nn.gelu(x, approximate=True)

def _silu(x):
    return jax.nn.silu(x)

def _sigmoid(x):
    return jax.nn.sigmoid(x)

def _layernorm(x, axis=-1, eps=1e-05):
    m = jnp.mean(x, axis=axis, keepdims=True)
    v = jnp.var(x, axis=axis, keepdims=True)
    return (x - m) / jnp.sqrt(v + eps)

def _scatter_add(tgt, idx, src, axis=0):
    return tgt.at[idx].add(src)

def _segment_sum(src, seg, n):
    return jax.ops.segment_sum(src, seg, n)
kernel_name = 'mk_dlrm_tower_d1_rec_r8_986b79'

def setup_inputs(seed: int=0):
    np.random.seed(seed)
    _w = jnp.asarray

    def _rec_inputs():
        import jax
        import jax.numpy as jnp
        _tk = jax.random.key(seed)
        ids = jnp.stack([jax.random.randint(jax.random.fold_in(_tk, 200 + f), (512,), 0, v, jnp.int32) for f, v in enumerate([1000, 12500, 1000, 1000, 125000, 1000, 12500, 1000, 12500, 12500, 1250, 1250, 1250, 1250, 12500, 1250, 1250, 1000, 12500, 1250, 1000, 1250, 12500, 1250, 1000, 1000])], axis=1)
        tbl_0 = 0.05 * jax.random.normal(jax.random.fold_in(_tk, 500 + 0), (1000, 128), jnp.float32)
        tbl_1 = 0.05 * jax.random.normal(jax.random.fold_in(_tk, 500 + 1), (12500, 128), jnp.float32)
        tbl_2 = 0.05 * jax.random.normal(jax.random.fold_in(_tk, 500 + 2), (1000, 128), jnp.float32)
        tbl_3 = 0.05 * jax.random.normal(jax.random.fold_in(_tk, 500 + 3), (1000, 128), jnp.float32)
        tbl_4 = 0.05 * jax.random.normal(jax.random.fold_in(_tk, 500 + 4), (125000, 128), jnp.float32)
        tbl_5 = 0.05 * jax.random.normal(jax.random.fold_in(_tk, 500 + 5), (1000, 128), jnp.float32)
        tbl_6 = 0.05 * jax.random.normal(jax.random.fold_in(_tk, 500 + 6), (12500, 128), jnp.float32)
        tbl_7 = 0.05 * jax.random.normal(jax.random.fold_in(_tk, 500 + 7), (1000, 128), jnp.float32)
        tbl_8 = 0.05 * jax.random.normal(jax.random.fold_in(_tk, 500 + 8), (12500, 128), jnp.float32)
        tbl_9 = 0.05 * jax.random.normal(jax.random.fold_in(_tk, 500 + 9), (12500, 128), jnp.float32)
        tbl_10 = 0.05 * jax.random.normal(jax.random.fold_in(_tk, 500 + 10), (1250, 128), jnp.float32)
        tbl_11 = 0.05 * jax.random.normal(jax.random.fold_in(_tk, 500 + 11), (1250, 128), jnp.float32)
        tbl_12 = 0.05 * jax.random.normal(jax.random.fold_in(_tk, 500 + 12), (1250, 128), jnp.float32)
        tbl_13 = 0.05 * jax.random.normal(jax.random.fold_in(_tk, 500 + 13), (1250, 128), jnp.float32)
        tbl_14 = 0.05 * jax.random.normal(jax.random.fold_in(_tk, 500 + 14), (12500, 128), jnp.float32)
        tbl_15 = 0.05 * jax.random.normal(jax.random.fold_in(_tk, 500 + 15), (1250, 128), jnp.float32)
        tbl_16 = 0.05 * jax.random.normal(jax.random.fold_in(_tk, 500 + 16), (1250, 128), jnp.float32)
        tbl_17 = 0.05 * jax.random.normal(jax.random.fold_in(_tk, 500 + 17), (1000, 128), jnp.float32)
        tbl_18 = 0.05 * jax.random.normal(jax.random.fold_in(_tk, 500 + 18), (12500, 128), jnp.float32)
        tbl_19 = 0.05 * jax.random.normal(jax.random.fold_in(_tk, 500 + 19), (1250, 128), jnp.float32)
        tbl_20 = 0.05 * jax.random.normal(jax.random.fold_in(_tk, 500 + 20), (1000, 128), jnp.float32)
        tbl_21 = 0.05 * jax.random.normal(jax.random.fold_in(_tk, 500 + 21), (1250, 128), jnp.float32)
        tbl_22 = 0.05 * jax.random.normal(jax.random.fold_in(_tk, 500 + 22), (12500, 128), jnp.float32)
        tbl_23 = 0.05 * jax.random.normal(jax.random.fold_in(_tk, 500 + 23), (1250, 128), jnp.float32)
        tbl_24 = 0.05 * jax.random.normal(jax.random.fold_in(_tk, 500 + 24), (1000, 128), jnp.float32)
        tbl_25 = 0.05 * jax.random.normal(jax.random.fold_in(_tk, 500 + 25), (1000, 128), jnp.float32)
        _rk = jax.random.fold_in(_tk, 7)
        r_dense_features = -0.000520686 + 1.00062 * jax.random.normal(jax.random.fold_in(_rk, 101), (512, 128), jnp.float32)
        W_top1 = 0.0405887 * jax.random.normal(jax.random.fold_in(_tk, 801), (607, 512), jnp.float32)
        W_top2 = 0.0441942 * jax.random.normal(jax.random.fold_in(_tk, 802), (512, 256), jnp.float32)
        W_top3 = 0.0625 * jax.random.normal(jax.random.fold_in(_tk, 803), (256, 1), jnp.float32)
        b_top1 = jnp.zeros((512,), jnp.float32)
        b_top2 = jnp.zeros((256,), jnp.float32)
        return (r_dense_features, ids, tbl_0, tbl_1, tbl_2, tbl_3, tbl_4, tbl_5, tbl_6, tbl_7, tbl_8, tbl_9, tbl_10, tbl_11, tbl_12, tbl_13, tbl_14, tbl_15, tbl_16, tbl_17, tbl_18, tbl_19, tbl_20, tbl_21, tbl_22, tbl_23, tbl_24, tbl_25, W_top1, b_top1, W_top2, b_top2, W_top3)
    r_dense_features, ids, tbl_0, tbl_1, tbl_2, tbl_3, tbl_4, tbl_5, tbl_6, tbl_7, tbl_8, tbl_9, tbl_10, tbl_11, tbl_12, tbl_13, tbl_14, tbl_15, tbl_16, tbl_17, tbl_18, tbl_19, tbl_20, tbl_21, tbl_22, tbl_23, tbl_24, tbl_25, W_top1, b_top1, W_top2, b_top2, W_top3 = _rec_inputs()

    def _L0_rec_setup():
        import jax, jax.numpy as jnp
        import numpy as np
        NUM_SPARSE = 26
        EMBED_DIM = 128
        BATCH = 2048
        key = jax.random.key(seed)
        k1, k2 = jax.random.split(key)
        dense_features = jax.random.normal(k1, (BATCH, EMBED_DIM), dtype=jnp.float32)
        sparse_features = jax.random.normal(k2, (BATCH, NUM_SPARSE, EMBED_DIM), dtype=jnp.float32)
        return {'dense_features': dense_features, 'sparse_features': sparse_features}
    _L0_rec_all = _L0_rec_setup()
    _L0_rec_in = {k: v for k, v in _L0_rec_all.items() if k in ()}
    del _L0_rec_all
    return {'r_dense_features': r_dense_features, 'ids': ids, 'tbl_0': tbl_0, 'tbl_1': tbl_1, 'tbl_2': tbl_2, 'tbl_3': tbl_3, 'tbl_4': tbl_4, 'tbl_5': tbl_5, 'tbl_6': tbl_6, 'tbl_7': tbl_7, 'tbl_8': tbl_8, 'tbl_9': tbl_9, 'tbl_10': tbl_10, 'tbl_11': tbl_11, 'tbl_12': tbl_12, 'tbl_13': tbl_13, 'tbl_14': tbl_14, 'tbl_15': tbl_15, 'tbl_16': tbl_16, 'tbl_17': tbl_17, 'tbl_18': tbl_18, 'tbl_19': tbl_19, 'tbl_20': tbl_20, 'tbl_21': tbl_21, 'tbl_22': tbl_22, 'tbl_23': tbl_23, 'tbl_24': tbl_24, 'tbl_25': tbl_25, 'W_top1': W_top1, 'b_top1': b_top1, 'W_top2': W_top2, 'b_top2': b_top2, 'W_top3': W_top3}

def reference(r_dense_features, ids, tbl_0, tbl_1, tbl_2, tbl_3, tbl_4, tbl_5, tbl_6, tbl_7, tbl_8, tbl_9, tbl_10, tbl_11, tbl_12, tbl_13, tbl_14, tbl_15, tbl_16, tbl_17, tbl_18, tbl_19, tbl_20, tbl_21, tbl_22, tbl_23, tbl_24, tbl_25, W_top1, b_top1, W_top2, b_top2, W_top3):
    import jax
    import jax.numpy as jnp

    def _L0_rec_ref(dense_features, sparse_features):
        import jax, jax.numpy as jnp
        import numpy as np
        NUM_SPARSE = 26
        EMBED_DIM = 128
        BATCH = 2048
        F = NUM_SPARSE + 1
        combined = jnp.concatenate([dense_features[:, None, :], sparse_features], axis=1)
        interactions = jnp.einsum('bfd,bgd->bfg', combined, combined)
        iu, ju = jnp.triu_indices(F, k=1)
        interactions_flat = interactions[:, iu, ju]
        return jnp.concatenate([dense_features, interactions_flat], axis=1)
    e = jnp.stack([tbl_0[ids[:, 0]], tbl_1[ids[:, 1]], tbl_2[ids[:, 2]], tbl_3[ids[:, 3]], tbl_4[ids[:, 4]], tbl_5[ids[:, 5]], tbl_6[ids[:, 6]], tbl_7[ids[:, 7]], tbl_8[ids[:, 8]], tbl_9[ids[:, 9]], tbl_10[ids[:, 10]], tbl_11[ids[:, 11]], tbl_12[ids[:, 12]], tbl_13[ids[:, 13]], tbl_14[ids[:, 14]], tbl_15[ids[:, 15]], tbl_16[ids[:, 16]], tbl_17[ids[:, 17]], tbl_18[ids[:, 18]], tbl_19[ids[:, 19]], tbl_20[ids[:, 20]], tbl_21[ids[:, 21]], tbl_22[ids[:, 22]], tbl_23[ids[:, 23]], tbl_24[ids[:, 24]], tbl_25[ids[:, 25]]], axis=1)
    z = _L0_rec_ref(r_dense_features, e)
    z = z.reshape(z.shape[0], -1)
    h = jnp.concatenate([z, r_dense_features], axis=1)
    h = jnp.maximum(h @ W_top1 + b_top1, 0.0)
    h = jnp.maximum(h @ W_top2 + b_top2, 0.0)
    y = h @ W_top3
    return y

_drawn_inputs = setup_inputs


def setup_inputs(seed=0):
    import zlib

    import numpy as np

    out = dict(_drawn_inputs(seed))
    spreads = {'b_top1': (0.0, 0.1), 'b_top2': (0.0, 0.1)}
    factors = {}
    for name, (base, spread) in spreads.items():
        noise = np.random.default_rng([zlib.crc32(name.encode()), seed]).standard_normal(out[name].shape)
        drawn = base * np.exp(spread * noise) if base else spread * noise
        out[name] = jnp.asarray(drawn.astype(out[name].dtype))
    for name, factor in factors.items():
        out[name] = (out[name] * factor).astype(out[name].dtype)
    return out
```

```python
from contextlib import ExitStack

import concourse.bass as bass
from concourse import mybir

F32 = mybir.dt.float32
I32 = mybir.dt.int32
U32 = mybir.dt.uint32
ALU = mybir.AluOpType
ACT = mybir.ActivationFunctionType

P = 128
Q = 32
QUADS = P // Q
SLOTS = 32
GROUP = 4
BANKS = 2
PASSES = ((0, 16), (16, 28))


def chunks(g0, g1):
    return (g1 - g0) // QUADS


def pair_place(f, g):
    chunk0 = 0
    for g0, g1 in PASSES:
        if g < g1:
            return SLOTS * ((g - g0) // chunks(g0, g1)) + f, chunk0 + (g - g0) % chunks(g0, g1)
        chunk0 += chunks(g0, g1)


def dlrm_tower(nc, dense, ids, tables, w1_dense, w1_pairs, w2, vectors, out):
    B, D = dense.shape
    F = len(tables) + 1
    TILES = B // P
    N1, N2 = w1_dense.shape[2], w2.shape[2]
    C1, C2 = N1 // P, N2 // P
    FIRST, SECOND = PASSES
    CF, CS = chunks(*FIRST), chunks(*SECOND)
    WIDE = QUADS * (FIRST[1] - FIRST[0])
    GROUPS = [range(k, min(k + GROUP, F)) for k in range(0, F, GROUP)]
    NG = len(GROUPS)
    FIRST_GROUPS = FIRST[1] // GROUP
    PAR = 2
    STEPS = TILES // PAR
    assert C1 == 4 and C2 == 2 and D == P and TILES % PAR == 0 and PAR * NG % BANKS == 0

    ids_rows = ids.rearrange("(p t) f -> p t f", t=TILES)
    dense_rows = dense.rearrange("(p t) d -> p t d", t=TILES)

    with ExitStack() as ctx:
        def sb(name, shape, dt=F32):
            return ctx.enter_context(nc.sbuf_tensor(name, shape, dt))

        def ps(name, shape):
            return ctx.enter_context(nc.psum_tensor(name, shape, F32))

        def sem(name):
            return ctx.enter_context(nc.semaphore(name))

        ids_sb = sb("ids_sb", [P, PAR, F - 1], I32)
        rows = sb("rows", [P, PAR, F, D])
        cols = sb("cols", [P, PAR, P, SLOTS])
        pairs = sb("pairs", [P, PAR, CF + CS, P])
        identity = sb("identity", [P, P])
        w1d = sb("w1d", [P, 2, N1])
        w1ds = sb("w1ds", [P, N1])
        w1p = sb("w1p", [P, CF + CS, N1])
        w2s = sb("w2s", [P, C1, N2])
        vec = sb("vec", [P, C1 + C2 + C2])
        h1 = sb("h1", [P, C1, P])
        h2 = sb("h2", [P, C2, P])
        y = sb("y", [1, B])
        b1, b2, w3 = vec[:, 0:C1], vec[:, C1:C1 + C2], vec[:, C1 + C2:C1 + 2 * C2]
        y_tiles = y[:, :].rearrange("o (q k i r) -> o i r k q", k=QUADS, i=STEPS, r=PAR)

        turned = ps("turned", [P, BANKS, GROUP, P])
        gram = ps("gram", [P, Q, WIDE])
        layer_ps = ps("layer_ps", [P, 2, 4 * P])
        h1_ps = [layer_ps[:, n // 2, n % 2 * P:(n % 2 + 1) * P] for n in range(C1)]
        h2_ps = [layer_ps[:, m, 2 * P:3 * P] for m in range(C2)]
        y_ps = layer_ps[0:1, 0, 3 * P:4 * P]

        ids_landed = [sem(f"ids_landed{r}") for r in range(PAR)]
        dense_landed = [sem(f"dense_landed{r}") for r in range(PAR)]
        gathered = [[sem(f"gathered{r}_{k}") for k in range(NG)] for r in range(PAR)]
        w1d_landed = sem("w1d_landed")
        w1p_landed = sem("w1p_landed")
        w2_landed = sem("w2_landed")
        vec_landed = sem("vec_landed")
        identity_zeroed = sem("identity_zeroed")
        identity_ready = sem("identity_ready")
        cols_zeroed = sem("cols_zeroed")
        w1d_summed = sem("w1d_summed")
        rows_free = [sem(f"rows_free{r}") for r in range(PAR)]
        group_turned = [sem(f"group_turned{b}") for b in range(BANKS)]
        group_copied = [sem(f"group_copied{b}") for b in range(BANKS)]
        first_done = sem("first_done")
        first_moved = [sem(f"first_moved_{e}") for e in ("act", "dve")]
        second_done = [sem(f"second_done_half{h}") for h in range(2)]
        second_moved = [sem(f"second_moved_{e}") for e in ("act", "dve")]
        layers_free = sem("layers_free")
        h1_done = [sem(f"h1_done_{e}") for e in ("act", "dve")]
        h1_relued = [sem(f"h1_relued_{e}") for e in ("act", "dve")]
        h2_done = [sem(f"h2_done_{e}") for e in ("act", "dve")]
        h2_relued = [sem(f"h2_relued_{e}") for e in ("act", "dve")]
        y_done = sem("y_done")
        y_stored = sem("y_stored")

        def bank(r, k):
            return (r * NG + k) % BANKS

        def uses(i, r, k, b):
            return i * (PAR * NG // BANKS) + (r * NG + k + BANKS - 1 - b) // BANKS

        def tile_count(i, r):
            return i * PAR + (r + 1)

        block = ctx.enter_context(nc.Block())

        @block.sync
        def _(sp):
            with sp.Fori(0, STEPS) as i:
                for r in range(PAR):
                    sp.wait_ge(rows_free[r], i + 1)
                    sp.dma_start(ids_sb[:, r, :], ids_rows[:, i * PAR + r, :]).then_inc(ids_landed[r], 16)
                    sp.dma_start(rows[:, r, 0, :], dense_rows[:, i * PAR + r, :]).then_inc(dense_landed[r], 16)
            sp.wait_ge(layers_free, TILES + 1)
            sp.dma_start(out.rearrange("b o -> o b"), y[:]).then_inc(y_stored, 16)
            sp.wait_ge(y_stored, 16)

        @block.gpsimd
        def _(pool):
            pool.memset(identity[:], 0.0).then_inc(identity_zeroed, 1)
            pool.wait_ge(identity_zeroed, 1)
            pool.affine_select(out=identity[:], in_=identity[:], compare_op=ALU.not_equal, fill=1.0, base=0,
                               pattern=[[-1, P]], channel_multiplier=1).then_inc(identity_ready, 1)
            with pool.Fori(0, STEPS) as i:
                for r in range(PAR):
                    pool.wait_ge(rows_free[r], i + 1)
                    pool.wait_ge(ids_landed[r], (i + 1) * 16)
                    pool.nop(nofuse=True)
                    for k in range(NG):
                        for f in GROUPS[k]:
                            if f > 0:
                                pool.indirect_dma_start(
                                    rows[:, r, f, :], None, tables[f - 1], bass.IndirectOffsetOnAxis(
                                        ap=ids_sb[:, r, f - 1:f].bitcast(U32), axis=0)
                                ).then_inc(gathered[r][k], 16)

        @block.tensor
        def _(pe):
            def transposes(i, r, k):
                b = bank(r, k)
                if k == 0:
                    pe.wait_ge(dense_landed[r], (i + 1) * 16)
                n_gathers = len(GROUPS[k]) - (k == 0)
                pe.wait_ge(gathered[r][k], (i + 1) * (16 * n_gathers))
                if k >= BANKS:
                    pe.wait_ge(group_copied[b], uses(i, r, k, b))
                for n, f in enumerate(GROUPS[k]):
                    last = pe.transpose(turned[:, b, n, :], rows[:, r, f, :], identity[:])
                last.then_inc(group_turned[b], 1)

            def gram_of(r, q, g0, g1):
                four = cols[:, r, QUADS * q:QUADS * (q + 1), :]
                return pe.matmul(gram[:, q, 0:QUADS * (g1 - g0)], four.rearrange("d k f -> d (k f)"),
                                 four[:, :, g0:g1], start=True, stop=True)

            def layer1(r, n, weights, rhs, start, stop):
                return pe.matmul(h1_ps[n], weights[:, n * P:(n + 1) * P], rhs,
                                 start=start and n % 2 == 0, stop=stop, skip_group_check=True)

            pe.wait_ge(identity_ready, 1)
            with pe.Fori(0, STEPS) as i:
                for r in range(PAR):
                    for k in range(FIRST_GROUPS):
                        transposes(i, r, k)

                    for b in range(BANKS):
                        pe.wait_ge(group_copied[b], uses(i, r, FIRST_GROUPS, b))
                    for q in range(Q):
                        last = gram_of(r, q, *FIRST)
                    last.then_inc(first_done, 1)

                    transposes(i, r, FIRST_GROUPS)

                    pe.wait_ge(w1d_summed, 1)
                    pe.wait_ge(w1p_landed, 16)
                    pe.wait_ge(layers_free, tile_count(i, r))
                    for n in range(C1):
                        layer1(r, n, w1ds, cols[:, r, :, 0].rearrange("d (q k) -> d k q", k=QUADS), True, False)
                    for moved in first_moved:
                        pe.wait_ge(moved, tile_count(i, r))
                    for c in range(CF):
                        for n in range(C1):
                            layer1(r, n, w1p[:, c, :], pairs[:, r, c, :], False, False)

                    for k in range(FIRST_GROUPS + 1, NG):
                        transposes(i, r, k)

                    for b in range(BANKS):
                        pe.wait_ge(group_copied[b], uses(i, r, NG, b))
                    for half in range(2):
                        for q in range(half * Q // 2, (half + 1) * Q // 2):
                            last = gram_of(r, q, *SECOND)
                            if q == 0:
                                last.then_inc(rows_free[r], 1)
                        last.then_inc(second_done[half], 1)

                    for moved in second_moved:
                        pe.wait_ge(moved, tile_count(i, r))
                    for c in range(CF, CF + CS):
                        for n in range(C1):
                            last = layer1(r, n, w1p[:, c, :], pairs[:, r, c, :], False, c == CF + CS - 1)
                            if c == CF + CS - 1 and n % 2 == 1:
                                last.then_inc(h1_done[n // 2], 1)

                    pe.wait_ge(w2_landed, 16)
                    for m in range(C2):
                        for n in range(C1):
                            if m == 0 and n % 2 == 0:
                                pe.wait_ge(h1_relued[n // 2], tile_count(i, r))
                            last = pe.matmul(h2_ps[m], w2s[:, n, m * P:(m + 1) * P], h1[:, n, :],
                                             start=(n == 0), stop=(n == C1 - 1))
                        last.then_inc(h2_done[m], 1)

                    pe.wait_ge(vec_landed, 16)
                    for m in range(C2):
                        pe.wait_ge(h2_relued[m], tile_count(i, r))
                        last = pe.matmul(y_ps, w3[:, m:m + 1], h2[:, m, :], start=(m == 0), stop=(m == C2 - 1))
                    last.then_inc(y_done, 1)

        def copy_group(eng, copy, i, r, k):
            b = bank(r, k)
            eng.wait_ge(group_turned[b], uses(i, r, k, b) + 1)
            if k >= FIRST_GROUPS:
                eng.wait_ge(first_done, tile_count(i, r))
            f0, n = GROUPS[k][0], len(GROUPS[k])
            copy(cols[:, r, :, f0:f0 + n].rearrange("d b f -> d f b"),
                 turned[:, b, 0:n, :]).then_inc(group_copied[b], 1)

        def move(copy, r, quads, q0, q1, g0, g1, c0):
            nc_ = chunks(g0, g1)
            for quad in quads:
                for j in range(QUADS):
                    g = quad * (g1 - g0) + nc_ * j
                    last = copy(pairs[Q * j:Q * (j + 1), r, c0:c0 + nc_, Q * quad + q0:Q * quad + q1],
                                gram[Q * quad:Q * (quad + 1), q0:q1, g:g + nc_].rearrange("f q c -> f c q"))
            return last

        def regroup(eng, copy, i, r, e):
            quads = (2 * e, 2 * e + 1)
            for k in range(FIRST_GROUPS):
                if bank(r, k) == e:
                    copy_group(eng, copy, i, r, k)
            eng.wait_ge(first_done, tile_count(i, r))
            move(copy, r, quads, 0, Q, *FIRST, 0).then_inc(first_moved[e], 1)
            for k in range(FIRST_GROUPS, NG):
                if bank(r, k) == e:
                    copy_group(eng, copy, i, r, k)
            for half in range(2):
                eng.wait_ge(second_done[half], tile_count(i, r))
                last = move(copy, r, quads, half * Q // 2, (half + 1) * Q // 2, *SECOND, CF)
            last.then_inc(second_moved[e], 1)

        @block.scalar
        def _(act):
            act.dma_start(w1d[:], w1_dense).then_inc(w1d_landed, 16)
            act.dma_start(w1p[:], w1_pairs).then_inc(w1p_landed, 16)
            act.dma_start(vec[:], vectors).then_inc(vec_landed, 16)
            act.dma_start(w2s[:], w2).then_inc(w2_landed, 16)
            act.wait_ge(vec_landed, 16)
            act.wait_ge(cols_zeroed, PAR)
            with act.Fori(0, STEPS) as i:
                for r in range(PAR):
                    regroup(act, act.copy, i, r, 0)
                    act.wait_ge(h1_done[0], tile_count(i, r))
                    for n in range(2):
                        last = act.activation(h1[:, n, :], h1_ps[n], ACT.Relu, bias=b1[:, n:n + 1])
                    last.then_inc(h1_relued[0], 1)
                    act.wait_ge(h2_done[0], tile_count(i, r))
                    act.activation(h2[:, 0, :], h2_ps[0], ACT.Relu, bias=b2[:, 0:1]).then_inc(h2_relued[0], 1)

        @block.vector
        def _(dve):
            dve.memset(y[:], 0.0).then_inc(layers_free, 1)
            for r in range(PAR):
                dve.memset(ids_sb[:, r, :], 0).then_inc(rows_free[r], 1)
            for r in range(PAR):
                dve.memset(cols[:, r], 0.0).then_inc(cols_zeroed, 1)
            dve.wait_ge(w1d_landed, 16)
            dve.tensor_tensor(w1ds[:], w1d[:, 0, :], w1d[:, 1, :], ALU.add).then_inc(w1d_summed, 1)
            dve.wait_ge(vec_landed, 16)
            dve.wait_ge(cols_zeroed, PAR)
            with dve.Fori(0, STEPS) as i:
                for r in range(PAR):
                    regroup(dve, dve.tensor_copy, i, r, 1)
                    dve.wait_ge(h1_done[1], tile_count(i, r))
                    for n in range(2, C1):
                        last = dve.tensor_scalar(h1[:, n, :], h1_ps[n], b1[:, n:n + 1], 0.0, ALU.add, ALU.max)
                    last.then_inc(h1_relued[1], 1)
                    dve.wait_ge(h2_done[1], tile_count(i, r))
                    dve.tensor_scalar(h2[:, 1, :], h2_ps[1], b2[:, 1:2], 0.0, ALU.add,
                                      ALU.max).then_inc(h2_relued[1], 1)
                    dve.wait_ge(y_done, tile_count(i, r))
                    dve.tensor_copy(y_tiles[:, i, r, :, :],
                                    y_ps.rearrange("o (k q) -> o k q", k=QUADS)).then_inc(layers_free, 1)


def kernel(**inputs):
    import numpy as np
    import concourse.bacc as bacc
    from concourse.bass_utils import run_bass_kernel_spmd

    a = {k: np.ascontiguousarray(v) for k, v in inputs.items()}
    dense, ids = a["r_dense_features"], a["ids"]
    tables = [a[f"tbl_{n}"] for n in range(ids.shape[1])]
    w1, w2, w3 = a["W_top1"], a["W_top2"], a["W_top3"]
    D, F, N1 = dense.shape[1], len(tables) + 1, w1.shape[1]

    w1_dense = np.ascontiguousarray(np.stack([w1[:D], w1[-D:]], axis=1))
    w1_pairs = np.zeros((P, sum(chunks(*p) for p in PASSES), N1), w1.dtype)
    row = D
    for f in range(F):
        for g in range(f + 1, F):
            w1_pairs[pair_place(f, g)] = w1[row]
            row += 1
    arrays = {
        "dense": dense, "ids": ids,
        **{f"table{n}": t for n, t in enumerate(tables)},
        "w1_dense": w1_dense, "w1_pairs": w1_pairs,
        "w2": np.ascontiguousarray(w2.reshape(N1 // P, P, -1).transpose(1, 0, 2)),
        "vectors": np.concatenate([v.reshape(-1, P).T for v in (a["b_top1"], a["b_top2"], w3)], axis=1),
    }
    nc = bacc.Bacc("TRN2", target_bir_lowering=False, num_devices=1)
    ap = {k: nc.dram_tensor(k, v.shape, mybir.dt.from_np(v.dtype), kind="ExternalInput").ap()
          for k, v in arrays.items()}
    out = nc.dram_tensor("out", (dense.shape[0], 1), F32, kind="ExternalOutput").ap()
    dlrm_tower(nc, ap["dense"], ap["ids"], [ap[f"table{n}"] for n in range(len(tables))],
               ap["w1_dense"], ap["w1_pairs"], ap["w2"], ap["vectors"], out)
    arrays = {k: np.ascontiguousarray(v) for k, v in arrays.items()}
    return run_bass_kernel_spmd(nc, [arrays], core_ids=[0]).results[0]["out"]
```

```python
from contextlib import ExitStack

import concourse.bass as bass
from concourse import mybir

F32 = mybir.dt.float32
I32 = mybir.dt.int32
U32 = mybir.dt.uint32
ALU = mybir.AluOpType
ACT = mybir.ActivationFunctionType

P = 128
Q = 32
QUADS = P // Q
SLOTS = 32
GROUP = 4
BANKS = 2
PASSES = ((0, 16), (16, 28))


def chunks(g0, g1):
    return (g1 - g0) // QUADS


def pair_place(f, g):
    chunk0 = 0
    for g0, g1 in PASSES:
        if g < g1:
            return SLOTS * ((g - g0) // chunks(g0, g1)) + f, chunk0 + (g - g0) % chunks(g0, g1)
        chunk0 += chunks(g0, g1)


def dlrm_tower(nc, dense, ids, tables, w1_dense, w1_pairs, w2, vectors, out):
    B, D = dense.shape
    F = len(tables) + 1
    TILES = B // P
    N1, N2 = w1_dense.shape[2], w2.shape[2]
    C1, C2 = N1 // P, N2 // P
    FIRST, SECOND = PASSES
    CF, CS = chunks(*FIRST), chunks(*SECOND)
    WIDE = QUADS * (FIRST[1] - FIRST[0])
    GROUPS = [range(k, min(k + GROUP, F)) for k in range(0, F, GROUP)]
    NG = len(GROUPS)
    UNITS = 4
    UQ = Q // UNITS
    FIRST_GROUPS = FIRST[1] // GROUP
    PAR = 2
    STEPS = TILES // PAR
    assert C1 == 4 and C2 == 2 and D == P and TILES % PAR == 0 and PAR * NG % BANKS == 0

    ids_rows = ids.rearrange("(p t) f -> p t f", t=TILES)
    dense_rows = dense.rearrange("(p t) d -> p t d", t=TILES)

    with ExitStack() as ctx:
        def sb(name, shape, dt=F32):
            return ctx.enter_context(nc.sbuf_tensor(name, shape, dt))

        def ps(name, shape):
            return ctx.enter_context(nc.psum_tensor(name, shape, F32))

        def sem(name):
            return ctx.enter_context(nc.semaphore(name))

        ids_sb = sb("ids_sb", [P, PAR, F - 1], I32)
        rows = sb("rows", [P, PAR, F, D])
        cols = sb("cols", [P, PAR, P, SLOTS])
        pairs = sb("pairs", [P, PAR, CF + CS, P])
        identity = sb("identity", [P, P])
        w1d = sb("w1d", [P, 2, N1])
        w1ds = sb("w1ds", [P, N1])
        w1p = sb("w1p", [P, CF + CS, N1])
        w2s = sb("w2s", [P, C1, N2])
        vec = sb("vec", [P, C1 + C2 + C2])
        h1 = sb("h1", [P, C1, P])
        h2 = sb("h2", [P, C2, P])
        y = sb("y", [1, B])
        b1, b2, w3 = vec[:, 0:C1], vec[:, C1:C1 + C2], vec[:, C1 + C2:C1 + 2 * C2]
        y_tiles = y[:, :].rearrange("o (q k i r) -> o i r k q", k=QUADS, i=STEPS, r=PAR)

        turned = ps("turned", [P, BANKS, GROUP, P])
        gram = ps("gram", [P, Q * WIDE])
        layer_ps = ps("layer_ps", [P, 2, 4 * P])
        h1_ps = [layer_ps[:, n // 2, n % 2 * P:(n % 2 + 1) * P] for n in range(C1)]
        h2_ps = [layer_ps[:, m, 2 * P:3 * P] for m in range(C2)]
        y_ps = layer_ps[0:1, 0, 3 * P:4 * P]

        ids_landed = [sem(f"ids_landed{r}") for r in range(PAR)]
        dense_landed = [sem(f"dense_landed{r}") for r in range(PAR)]
        gathered = [[sem(f"gathered{r}_{k}") for k in range(NG)] for r in range(PAR)]
        w1d_landed = sem("w1d_landed")
        w1p_landed = sem("w1p_landed")
        w2_landed = sem("w2_landed")
        vec_landed = sem("vec_landed")
        identity_zeroed = sem("identity_zeroed")
        identity_ready = sem("identity_ready")
        cols_zeroed = sem("cols_zeroed")
        w1d_summed = sem("w1d_summed")
        rows_free = [sem(f"rows_free{r}") for r in range(PAR)]
        group_turned = [sem(f"group_turned{b}") for b in range(BANKS)]
        group_copied = [sem(f"group_copied{b}") for b in range(BANKS)]
        first_done = sem("first_done")
        first_moved = [sem(f"first_moved_{e}") for e in ("act", "dve")]
        second_done = [sem(f"second_done_half{h}") for h in range(2)]
        second_moved = [sem(f"second_moved_{e}") for e in ("act", "dve")]
        unit_done = sem("unit_done")
        unit_moved = [sem(f"unit_moved_{e}") for e in ("act", "dve")]
        layers_free = sem("layers_free")
        h1_done = [sem(f"h1_done_{e}") for e in ("act", "dve")]
        h1_relued = [sem(f"h1_relued_{e}") for e in ("act", "dve")]
        h2_done = [sem(f"h2_done_{e}") for e in ("act", "dve")]
        h2_relued = [sem(f"h2_relued_{e}") for e in ("act", "dve")]
        y_done = sem("y_done")
        y_stored = sem("y_stored")

        def bank(r, k):
            return (r * NG + k) % BANKS

        def uses(i, r, k, b):
            return i * (PAR * NG // BANKS) + (r * NG + k + BANKS - 1 - b) // BANKS

        def tile_count(i, r):
            return i * PAR + (r + 1)

        block = ctx.enter_context(nc.Block())

        @block.sync
        def _(sp):
            with sp.Fori(0, STEPS) as i:
                for r in range(PAR):
                    sp.wait_ge(rows_free[r], i + 1)
                    sp.dma_start(ids_sb[:, r, :], ids_rows[:, i * PAR + r, :]).then_inc(ids_landed[r], 16)
                    sp.dma_start(rows[:, r, 0, :], dense_rows[:, i * PAR + r, :]).then_inc(dense_landed[r], 16)
            sp.wait_ge(layers_free, TILES + 1)
            sp.dma_start(out.rearrange("b o -> o b"), y[:]).then_inc(y_stored, 16)
            sp.wait_ge(y_stored, 16)

        @block.gpsimd
        def _(pool):
            pool.memset(identity[:], 0.0).then_inc(identity_zeroed, 1)
            pool.wait_ge(identity_zeroed, 1)
            pool.affine_select(out=identity[:], in_=identity[:], compare_op=ALU.not_equal, fill=1.0, base=0,
                               pattern=[[-1, P]], channel_multiplier=1).then_inc(identity_ready, 1)
            with pool.Fori(0, STEPS) as i:
                for r in range(PAR):
                    pool.wait_ge(rows_free[r], i + 1)
                    pool.wait_ge(ids_landed[r], (i + 1) * 16)
                    pool.nop(nofuse=True)
                    for k in range(NG):
                        for f in GROUPS[k]:
                            if f > 0:
                                pool.indirect_dma_start(
                                    rows[:, r, f, :], None, tables[f - 1], bass.IndirectOffsetOnAxis(
                                        ap=ids_sb[:, r, f - 1:f].bitcast(U32), axis=0)
                                ).then_inc(gathered[r][k], 16)

        @block.tensor
        def _(pe):
            def transposes(i, r, k):
                b = bank(r, k)
                if k == 0:
                    pe.wait_ge(dense_landed[r], (i + 1) * 16)
                n_gathers = len(GROUPS[k]) - (k == 0)
                pe.wait_ge(gathered[r][k], (i + 1) * (16 * n_gathers))
                if k >= BANKS:
                    pe.wait_ge(group_copied[b], uses(i, r, k, b))
                for n, f in enumerate(GROUPS[k]):
                    last = pe.transpose(turned[:, b, n, :], rows[:, r, f, :], identity[:])
                last.then_inc(group_turned[b], 1)

            def gram_of(r, q, slot, g0, g1):
                four = cols[:, r, QUADS * q:QUADS * (q + 1), :]
                n = QUADS * (g1 - g0)
                return pe.matmul(gram[:, slot:slot + n], four.rearrange("d k f -> d (k f)"),
                                 four[:, :, g0:g1], start=True, stop=True)

            def layer1(r, n, weights, rhs, start=False, stop=False):
                return pe.matmul(h1_ps[n], weights[:, n * P:(n + 1) * P], rhs,
                                 start=start and n % 2 == 0, stop=stop, skip_group_check=True)

            def layer1_dense(i, r):
                pe.wait_ge(w1d_summed, 1)
                pe.wait_ge(layers_free, tile_count(i, r))
                for n in range(C1):
                    layer1(r, n, w1ds, cols[:, r, :, 0].rearrange("d (q k) -> d k q", k=QUADS), start=True)

            def layer1_pairs(r, c0, c1):
                pe.wait_ge(w1p_landed, 16)
                for c in range(c0, c1):
                    for n in range(C1):
                        last = layer1(r, n, w1p[:, c, :], pairs[:, r, c, :], stop=(c == CF + CS - 1))
                        if c == CF + CS - 1 and n % 2 == 1:
                            last.then_inc(h1_done[n // 2], 1)

            def gram_whole(i, r):
                for k in range(NG):
                    transposes(i, r, k)
                for b in range(BANKS):
                    pe.wait_ge(group_copied[b], uses(i, r, NG, b))
                for u in range(UNITS):
                    if u >= 2:
                        for moved in unit_moved:
                            pe.wait_ge(moved, i * UNITS + (u - 1))
                    for q in range(u * UQ, (u + 1) * UQ):
                        last = gram_of(r, q, q % (2 * UQ) * P, 0, SECOND[1])
                        if q == 0:
                            last.then_inc(rows_free[r], 1)
                    last.then_inc(unit_done, 1)
                layer1_dense(i, r)
                for moved in unit_moved:
                    pe.wait_ge(moved, (i + 1) * UNITS)
                layer1_pairs(r, 0, CF + CS)

            def gram_in_passes(i, r):
                for k in range(FIRST_GROUPS):
                    transposes(i, r, k)
                for b in range(BANKS):
                    pe.wait_ge(group_copied[b], uses(i, r, FIRST_GROUPS, b))
                for q in range(Q):
                    last = gram_of(r, q, q * WIDE, *FIRST)
                last.then_inc(first_done, 1)
                transposes(i, r, FIRST_GROUPS)
                layer1_dense(i, r)
                for moved in first_moved:
                    pe.wait_ge(moved, i + 1)
                layer1_pairs(r, 0, CF)
                for k in range(FIRST_GROUPS + 1, NG):
                    transposes(i, r, k)
                for b in range(BANKS):
                    pe.wait_ge(group_copied[b], uses(i, r, NG, b))
                for half in range(2):
                    for q in range(half * Q // 2, (half + 1) * Q // 2):
                        last = gram_of(r, q, q * WIDE, *SECOND)
                        if q == 0:
                            last.then_inc(rows_free[r], 1)
                    last.then_inc(second_done[half], 1)
                for moved in second_moved:
                    pe.wait_ge(moved, i + 1)
                layer1_pairs(r, CF, CF + CS)

            pe.wait_ge(identity_ready, 1)
            with pe.Fori(0, STEPS) as i:
                for r in range(PAR):
                    if r == 0:
                        gram_whole(i, r)
                    else:
                        gram_in_passes(i, r)

                    pe.wait_ge(w2_landed, 16)
                    for m in range(C2):
                        for n in range(C1):
                            if m == 0 and n % 2 == 0:
                                pe.wait_ge(h1_relued[n // 2], tile_count(i, r))
                            last = pe.matmul(h2_ps[m], w2s[:, n, m * P:(m + 1) * P], h1[:, n, :],
                                             start=(n == 0), stop=(n == C1 - 1))
                        last.then_inc(h2_done[m], 1)

                    pe.wait_ge(vec_landed, 16)
                    for m in range(C2):
                        pe.wait_ge(h2_relued[m], tile_count(i, r))
                        last = pe.matmul(y_ps, w3[:, m:m + 1], h2[:, m, :], start=(m == 0), stop=(m == C2 - 1))
                    last.then_inc(y_done, 1)

        def copy_group(eng, copy, i, r, k):
            b = bank(r, k)
            eng.wait_ge(group_turned[b], uses(i, r, k, b) + 1)
            f0, n = GROUPS[k][0], len(GROUPS[k])
            copy(cols[:, r, :, f0:f0 + n].rearrange("d b f -> d f b"),
                 turned[:, b, 0:n, :]).then_inc(group_copied[b], 1)

        def move(copy, r, quads, q0, q1, products, g0, g1, c0):
            n = chunks(g0, g1)
            for quad in quads:
                for j in range(QUADS):
                    last = copy(pairs[Q * j:Q * (j + 1), r, c0:c0 + n, Q * quad + q0:Q * quad + q1],
                                products[Q * quad:Q * (quad + 1), :, quad, n * j:n * (j + 1)]
                                .rearrange("f q c -> f c q"))
            return last

        def regroup_whole(eng, copy, i, r, e):
            quads = (2 * e, 2 * e + 1)
            for k in range(NG):
                if bank(r, k) == e:
                    copy_group(eng, copy, i, r, k)
            for u in range(UNITS):
                eng.wait_ge(unit_done, i * UNITS + (u + 1))
                unit = gram[:, u % 2 * UQ * P:(u % 2 + 1) * UQ * P].rearrange("f (q n) -> f q n", n=P)
                unit = unit[:, :, 0:QUADS * SECOND[1]].rearrange("f q (k g) -> f q k g", k=QUADS)
                q0, q1 = u * UQ, (u + 1) * UQ
                move(copy, r, quads, q0, q1, unit[:, :, :, 0:FIRST[1]], *FIRST, 0)
                move(copy, r, quads, q0, q1, unit[:, :, :, FIRST[1]:SECOND[1]], *SECOND, CF).then_inc(unit_moved[e], 1)

        def regroup_in_passes(eng, copy, i, r, e):
            quads = (2 * e, 2 * e + 1)
            for k in range(FIRST_GROUPS):
                if bank(r, k) == e:
                    copy_group(eng, copy, i, r, k)
            eng.wait_ge(first_done, i + 1)
            products = gram[:, :].rearrange("f (q n) -> f q n", n=WIDE)
            move(copy, r, quads, 0, Q, products.rearrange("f q (k g) -> f q k g", k=QUADS),
                 *FIRST, 0).then_inc(first_moved[e], 1)
            for k in range(FIRST_GROUPS, NG):
                if bank(r, k) == e:
                    copy_group(eng, copy, i, r, k)
            narrow = products[:, :, 0:QUADS * (SECOND[1] - SECOND[0])].rearrange("f q (k g) -> f q k g", k=QUADS)
            for half in range(2):
                eng.wait_ge(second_done[half], i + 1)
                q0, q1 = half * Q // 2, (half + 1) * Q // 2
                last = move(copy, r, quads, q0, q1, narrow[:, q0:q1], *SECOND, CF)
            last.then_inc(second_moved[e], 1)

        @block.scalar
        def _(act):
            act.wait_ge(ids_landed[0], 16)
            act.dma_start(w1d[:], w1_dense).then_inc(w1d_landed, 16)
            act.dma_start(w1p[:], w1_pairs).then_inc(w1p_landed, 16)
            act.dma_start(vec[:], vectors).then_inc(vec_landed, 16)
            act.dma_start(w2s[:], w2).then_inc(w2_landed, 16)
            act.wait_ge(vec_landed, 16)
            act.wait_ge(cols_zeroed, PAR)
            with act.Fori(0, STEPS) as i:
                for r in range(PAR):
                    (regroup_whole if r == 0 else regroup_in_passes)(act, act.copy, i, r, 0)
                    act.wait_ge(h1_done[0], tile_count(i, r))
                    for n in range(2):
                        last = act.activation(h1[:, n, :], h1_ps[n], ACT.Relu, bias=b1[:, n:n + 1])
                    last.then_inc(h1_relued[0], 1)
                    act.wait_ge(h2_done[0], tile_count(i, r))
                    act.activation(h2[:, 0, :], h2_ps[0], ACT.Relu, bias=b2[:, 0:1]).then_inc(h2_relued[0], 1)

        @block.vector
        def _(dve):
            for r in range(PAR):
                dve.memset(ids_sb[:, r, 0:1], 0).then_inc(rows_free[r], 1)
            dve.memset(y[:, 0:1], 0.0).then_inc(layers_free, 1)
            for r in range(PAR):
                dve.memset(cols[:, r], 0.0).then_inc(cols_zeroed, 1)
            dve.wait_ge(w1d_landed, 16)
            dve.tensor_tensor(w1ds[:], w1d[:, 0, :], w1d[:, 1, :], ALU.add).then_inc(w1d_summed, 1)
            dve.wait_ge(vec_landed, 16)
            dve.wait_ge(cols_zeroed, PAR)
            with dve.Fori(0, STEPS) as i:
                for r in range(PAR):
                    (regroup_whole if r == 0 else regroup_in_passes)(dve, dve.tensor_copy, i, r, 1)
                    dve.wait_ge(h1_done[1], tile_count(i, r))
                    for n in range(2, C1):
                        last = dve.tensor_scalar(h1[:, n, :], h1_ps[n], b1[:, n:n + 1], 0.0, ALU.add, ALU.max)
                    last.then_inc(h1_relued[1], 1)
                    dve.wait_ge(h2_done[1], tile_count(i, r))
                    dve.tensor_scalar(h2[:, 1, :], h2_ps[1], b2[:, 1:2], 0.0, ALU.add,
                                      ALU.max).then_inc(h2_relued[1], 1)
                    dve.wait_ge(y_done, tile_count(i, r))
                    dve.tensor_copy(y_tiles[:, i, r, :, :],
                                    y_ps.rearrange("o (k q) -> o k q", k=QUADS)).then_inc(layers_free, 1)


def kernel(**inputs):
    import numpy as np
    import concourse.bacc as bacc
    from concourse.bass_utils import run_bass_kernel_spmd

    a = {k: np.ascontiguousarray(v) for k, v in inputs.items()}
    dense, ids = a["r_dense_features"], a["ids"]
    tables = [a[f"tbl_{n}"] for n in range(ids.shape[1])]
    w1, w2, w3 = a["W_top1"], a["W_top2"], a["W_top3"]
    D, F, N1 = dense.shape[1], len(tables) + 1, w1.shape[1]

    w1_dense = np.ascontiguousarray(np.stack([w1[:D], w1[-D:]], axis=1))
    w1_pairs = np.zeros((P, sum(chunks(*p) for p in PASSES), N1), w1.dtype)
    row = D
    for f in range(F):
        for g in range(f + 1, F):
            w1_pairs[pair_place(f, g)] = w1[row]
            row += 1
    arrays = {
        "dense": dense, "ids": ids,
        **{f"table{n}": t for n, t in enumerate(tables)},
        "w1_dense": w1_dense, "w1_pairs": w1_pairs,
        "w2": np.ascontiguousarray(w2.reshape(N1 // P, P, -1).transpose(1, 0, 2)),
        "vectors": np.concatenate([v.reshape(-1, P).T for v in (a["b_top1"], a["b_top2"], w3)], axis=1),
    }
    nc = bacc.Bacc("TRN2", target_bir_lowering=False, num_devices=1)
    ap = {k: nc.dram_tensor(k, v.shape, mybir.dt.from_np(v.dtype), kind="ExternalInput").ap()
          for k, v in arrays.items()}
    out = nc.dram_tensor("out", (dense.shape[0], 1), F32, kind="ExternalOutput").ap()
    dlrm_tower(nc, ap["dense"], ap["ids"], [ap[f"table{n}"] for n in range(len(tables))],
               ap["w1_dense"], ap["w1_pairs"], ap["w2"], ap["vectors"], out)
    arrays = {k: np.ascontiguousarray(v) for k, v in arrays.items()}
    return run_bass_kernel_spmd(nc, [arrays], core_ids=[0]).results[0]["out"]
```

```python
from contextlib import ExitStack

import concourse.bass as bass
from concourse import mybir

F32 = mybir.dt.float32
BF16 = mybir.dt.bfloat16
F16 = mybir.dt.float16
I32 = mybir.dt.int32
U32 = mybir.dt.uint32
ALU = mybir.AluOpType
ACT = mybir.ActivationFunctionType

P = 128
Q = 32
QUADS = P // Q
SLOTS = 32
BANK = 512
RESIDENT = 6
TABLES = 3
PARTS = 3
WARM = 8
GROUP = 4
BANKS = 2
CHUNKS = 7


def dlrm_tower(nc, dense, ids, small_ids, small, tables, w1_dense, w1_pairs, w2, vectors, out):
    B, D = dense.shape
    F = len(small) + 1 + len(tables)
    TILES = B // P
    N1, N2 = w1_dense.shape[2], w2.shape[2]
    C1, C2 = N1 // P, N2 // P
    G = QUADS * CHUNKS
    GROUPS = [range(g, min(g + GROUP, F)) for g in range(RESIDENT + 1, F, GROUP)]
    NG = len(GROUPS)
    UNITS = 4
    UQ = Q // UNITS
    LAST = TILES - 1
    V = small[0].shape[0]
    VP = next(p for p in range(P, 0, -1) if V % p == 0)
    VC = V // VP
    HALVES = slice(0, VC // 2), slice(VC // 2, VC)
    STAGES = 3 + C1
    assert C1 == 4 and C2 == 2 and D == P and F <= G <= SLOTS and UQ * 2 * G <= BANK
    assert TILES == GROUP and TILES * P <= BANK and V <= 2048 and NG > 4 and RESIDENT >= NG

    with ExitStack() as ctx:
        def sb(name, shape, dt=F32):
            return ctx.enter_context(nc.sbuf_tensor(name, shape, dt))

        def ps(name, shape):
            return ctx.enter_context(nc.psum_tensor(name, shape, F32))

        def sem(name):
            return ctx.enter_context(nc.semaphore(name))

        ids_sb = sb("ids_sb", [P, TILES, F - 1], I32)
        dense_sb = sb("dense_sb", [P, TILES, D])
        rows = sb("rows", [P, TILES, len(tables), D])
        cols = sb("cols", [P, TILES, P, SLOTS])
        pairs = sb("pairs", [P, 2, CHUNKS, P])
        identity = sb("identity", [P, P])
        table = sb("table", [VP, TABLES, VC, D])
        parts = sb("parts", [VP, TABLES, PARTS, VC, D], BF16)
        onehot = sb("onehot", [VP, 2, VC, TILES * P], BF16)
        ids_wide = sb("ids_wide", [P, 2, TILES * P], I32)
        ids16 = sb("ids16", [P, 2, TILES * P], F16)
        row_index = sb("row_index", [VP, VC], I32)
        row_number = sb("row_number", [VP, VC])
        w1d = sb("w1d", [P, 2, N1])
        w1ds = sb("w1ds", [P, N1])
        w1p = sb("w1p", [P, CHUNKS, N1])
        w2s = sb("w2s", [P, C1, N2])
        vec = sb("vec", [P, C1 + C2 + C2])
        h1 = sb("h1", [P, C1, P])
        h2 = sb("h2", [P, C2, P])
        y = sb("y", [1, B])
        b1, b2, w3 = vec[:, 0:C1], vec[:, C1:C1 + C2], vec[:, C1 + C2:C1 + 2 * C2]
        y_tiles = y[:, :].rearrange("o (q k t) -> o t k q", k=QUADS, t=TILES)

        turned = ps("turned", [P, BANKS, GROUP, P])
        gram = ps("gram", [P, 2, BANK])
        layer_ps = ps("layer_ps", [P, 4, BANK])
        found_ps = [gram[:, j, :] for j in range(2)]
        h1_ps = [layer_ps[:, n // 2, n % 2 * P:(n % 2 + 1) * P] for n in range(C1)]
        h2_ps = [layer_ps[:, 2 + m, 0:P] for m in range(C2)]
        y_ps = layer_ps[0:1, 2, P:2 * P]

        ids_landed = sem("ids_landed")
        dense_landed = sem("dense_landed")
        table_landed = [[sem(f"table_landed{j}_{h}") for h in range(2)] for j in range(RESIDENT)]
        row_index_ready = sem("row_index_ready")
        row_number_ready = sem("row_number_ready")
        wide_landed = [sem(f"wide_landed{j}") for j in range(RESIDENT)]
        ids16_ready = sem("ids16_ready")
        onehot_ready = sem("onehot_ready")
        high_ready = sem("high_ready")
        residue_ready = sem("residue_ready")
        middle_ready = sem("middle_ready")
        low_ready = sem("low_ready")
        found = sem("found")
        found_copied = sem("found_copied")
        gathered = [[sem(f"gathered{t}_{k}") for k in range(NG)] for t in range(TILES)]
        w1d_landed = sem("w1d_landed")
        w1p_landed = sem("w1p_landed")
        w2_landed = sem("w2_landed")
        vec_landed = sem("vec_landed")
        identity_zeroed = sem("identity_zeroed")
        identity_ready = sem("identity_ready")
        cols_zeroed = sem("cols_zeroed")
        w1d_summed = sem("w1d_summed")
        group_turned = [sem(f"group_turned{b}") for b in range(BANKS)]
        group_copied = [sem(f"group_copied{b}") for b in range(BANKS)]
        unit_done = sem("unit_done")
        unit_moved = [sem(f"unit_moved_{e}") for e in ("act", "dve")]
        h1_done = [sem(f"h1_done_{e}") for e in ("act", "dve")]
        h1_relued = [sem(f"h1_relued_{e}") for e in ("act", "dve")]
        h2_done = [sem(f"h2_done_{e}") for e in ("act", "dve")]
        h2_relued = [sem(f"h2_relued_{e}") for e in ("act", "dve")]
        y_done = sem("y_done")
        y_copied = sem("y_copied")
        y_stored = sem("y_stored")

        def bank(t, k):
            return (1 + t * NG + k) % BANKS

        def uses(t, k, b):
            return (1 + t * NG + k + BANKS - 1 - b) // BANKS

        def beside_lookup(j):
            k = j - (RESIDENT - NG + 1)
            return range(NG - 2, NG) if j == RESIDENT - 1 else range(k, k + 1) if k >= 0 else range(0)

        BEFORE_STAGES = range(2)

        def beside_stage(s, k):
            if s == LAST:
                return range(0)
            groups = {2: [2], 5: [3], 6: range(4, NG)}
            if s > 0:
                groups = {0: [0], 1: [1], 3: [2], 5: [3], 6: range(4, NG)}
            return groups.get(k, range(0))

        block = ctx.enter_context(nc.Block())

        @block.sync
        def _(sp):
            sp.dma_start(ids_sb[:], ids.rearrange("(p t) f -> p t f", t=TILES)).then_inc(ids_landed, 16)
            for j in range(RESIDENT):
                if j >= 2:
                    sp.wait_ge(ids16_ready, j - 1)
                sp.dma_start(ids_wide[:, j % 2],
                             small_ids[j:j + 1, :].to_broadcast([P, TILES * P])).then_inc(wide_landed[j], 16)
                if j >= TABLES:
                    sp.wait_ge(low_ready, 2 * (j - TABLES + 1))
                rows_of = small[j].rearrange("(p c) d -> p c d", c=VC)
                for h, cs in enumerate(HALVES):
                    for p0, p1 in ((0, VP // 16 * 16), (VP // 16 * 16, VP)):
                        sp.dma_start(table[p0:p1, j % TABLES, cs], rows_of[p0:p1, cs]).then_inc(table_landed[j][h], 16)
                if j == 1:
                    sp.dma_start(dense_sb[:], dense.rearrange("(p t) d -> p t d", t=TILES)).then_inc(dense_landed, 16)
            sp.wait_ge(found, 1)
            sp.dma_start(w1d[:], w1_dense).then_inc(w1d_landed, 16)
            sp.dma_start(vec[:], vectors).then_inc(vec_landed, 16)
            sp.dma_start(w1p[:], w1_pairs).then_inc(w1p_landed, 16)
            sp.dma_start(w2s[:], w2).then_inc(w2_landed, 16)
            sp.wait_ge(y_copied, TILES)
            sp.dma_start(out.rearrange("b o -> o b"), y[:]).then_inc(y_stored, 16)
            sp.wait_ge(y_stored, 16)

        @block.gpsimd
        def _(pool):
            pool.memset(identity[:], 0.0).then_inc(identity_zeroed, 1)
            pool.wait_ge(identity_zeroed, 1)
            pool.affine_select(out=identity[:], in_=identity[:], compare_op=ALU.not_equal, fill=1.0, base=0,
                               pattern=[[-1, P]], channel_multiplier=1).then_inc(identity_ready, 1)
            pool.iota(row_index[:], pattern=[[1, VC]], base=0, channel_multiplier=VC).then_inc(row_index_ready, 1)
            pool.wait_ge(ids_landed, 16)
            for t in range(TILES):
                for k in range(NG):
                    for f in GROUPS[k]:
                        n = f - RESIDENT - 1
                        pool.indirect_dma_start(
                            rows[:, t, n, :], None, tables[n], bass.IndirectOffsetOnAxis(
                                ap=ids_sb[:, t, f - 1:f].bitcast(U32), axis=0)
                        ).then_inc(gathered[t][k], 16)

        @block.tensor
        def _(pe):
            def transpose_dense():
                pe.wait_ge(dense_landed, 16)
                for t in range(TILES):
                    last = pe.transpose(turned[:, 0, t, :], dense_sb[:, t, :], identity[:])
                last.then_inc(group_turned[0], 1)

            def transposes(t, k):
                b = bank(t, k)
                pe.wait_ge(gathered[t][k], 16 * len(GROUPS[k]))
                if uses(t, k, b) > 0:
                    pe.wait_ge(group_copied[b], uses(t, k, b))
                for n, f in enumerate(GROUPS[k]):
                    last = pe.transpose(turned[:, b, n, :], rows[:, t, f - RESIDENT - 1, :], identity[:])
                last.then_inc(group_turned[b], 1)

            def look_up(j):
                if j >= 2:
                    pe.wait_ge(found_copied, j - 1)
                for part, ready in enumerate((high_ready, middle_ready, low_ready)):
                    for c in range(VC):
                        if c in (0, VC // 2):
                            pe.wait_ge(ready, 2 * j + 1 + (c > 0))
                        if part == 0:
                            pe.wait_ge(onehot_ready, VC * j + c + 1)
                        last = pe.matmul(found_ps[j % 2], parts[:, j % TABLES, part, c, :], onehot[:, j % 2, c, :],
                                         start=(part == 0 and c == 0), stop=(part == PARTS - 1 and c == VC - 1))
                last.then_inc(found, 1)

            def wait_for_cols(t, groups):
                for b in range(BANKS):
                    pe.wait_ge(group_copied[b], uses(t, groups, b))

            def gram_units(t, u0, u1):
                for u in range(u0, u1):
                    if UNITS * t + u >= 2:
                        for moved in unit_moved:
                            pe.wait_ge(moved, UNITS * t + u - 1)
                    for q in range(u * UQ, (u + 1) * UQ):
                        at = q % UQ * 2 * G
                        for k in (0, 2):
                            two = cols[:, t, QUADS * q + k:QUADS * q + k + 2, :]
                            last = pe.matmul(gram[Q * k:Q * (k + 2), u % 2, at:at + 2 * G],
                                             two.rearrange("d k f -> d (k f)"), two[:, :, 0:G],
                                             start=True, stop=True)
                    last.then_inc(unit_done, 1)

            def layer1(n, weights, rhs, start=False, stop=False):
                return pe.matmul(h1_ps[n], weights[:, n * P:(n + 1) * P], rhs,
                                 start=start and n % 2 == 0, stop=stop, skip_group_check=True)

            def layer1_dense(t):
                pe.wait_ge(w1d_summed, 1)
                for n in range(C1):
                    layer1(n, w1ds, cols[:, t, :, RESIDENT].rearrange("d (q k) -> d k q", k=QUADS), start=True)

            def layer1_pairs(t, n):
                pe.wait_ge(w1p_landed, 16)
                for c in range(CHUNKS):
                    last = layer1(n, w1p[:, c, :], pairs[:, t % 2, c, :], stop=(c == CHUNKS - 1))
                if n % 2 == 1:
                    last.then_inc(h1_done[n // 2], 1)

            def layer2(t, ms, ns):
                pe.wait_ge(w2_landed, 16)
                if t > 0:
                    pe.wait_ge(y_copied, t)
                for m in ms:
                    for n in ns:
                        if n % 2 == 0:
                            pe.wait_ge(h1_relued[n // 2], t + 1)
                        last = pe.matmul(h2_ps[m], w2s[:, n, m * P:(m + 1) * P], h1[:, n, :],
                                         start=(n == 0), stop=(n == C1 - 1))
                    if n == C1 - 1:
                        last.then_inc(h2_done[m], 1)

            def layer3(t):
                pe.wait_ge(vec_landed, 16)
                for m in range(C2):
                    pe.wait_ge(h2_relued[m], t + 1)
                    last = pe.matmul(y_ps, w3[:, m:m + 1], h2[:, m, :], start=(m == 0), stop=(m == C2 - 1))
                last.then_inc(y_done, 1)

            def stage(s, k):
                if k == 0:
                    if s == 0:
                        pe.wait_ge(cols_zeroed, 1)
                        pe.wait_ge(found_copied, RESIDENT)
                    if s > 0:
                        layer2(s - 1, [0], range(C1))
                    wait_for_cols(s, NG)
                    gram_units(s, 0, 2)
                if k == 1:
                    gram_units(s, 2, 4)
                if k == 2:
                    if s > 0:
                        layer2(s - 1, [1], range(C1))
                    layer1_dense(s)
                    if s > 0:
                        layer3(s - 1)
                if k == 3:
                    for moved in unit_moved:
                        pe.wait_ge(moved, UNITS * (s + 1))
                if k >= 3:
                    layer1_pairs(s, k - 3)

            pe.wait_ge(identity_ready, 1)
            for _ in range(WARM):
                pe.matmul(turned[:, 1, 0, :], identity[:], identity[:], start=True, stop=True)
            for j in range(RESIDENT):
                if j == 1:
                    transpose_dense()
                for k in beside_lookup(j):
                    transposes(0, k)
                look_up(j)
            for k in BEFORE_STAGES:
                transposes(1, k)
            for s in range(TILES):
                for k in range(STAGES):
                    stage(s, k)
                    for g in beside_stage(s, k):
                        transposes(s + 1, g)
            layer2(LAST, range(C2), range(2))
            layer2(LAST, range(C2), range(2, C1))
            layer3(LAST)

        def copy_dense(eng, copy):
            eng.wait_ge(group_turned[0], 1)
            copy(cols[:, :, :, RESIDENT], turned[:, 0, :, :]).then_inc(group_copied[0], 1)

        def copy_group(eng, copy, t, k):
            b = bank(t, k)
            eng.wait_ge(group_turned[b], uses(t, k, b) + 1)
            f0, n = GROUPS[k][0], len(GROUPS[k])
            copy(cols[:, t, :, f0:f0 + n].rearrange("d b f -> d f b"),
                 turned[:, b, 0:n, :]).then_inc(group_copied[b], 1)

        def move_units(eng, copy, t, e, u0, u1):
            for u in range(u0, u1):
                eng.wait_ge(unit_done, UNITS * t + u + 1)
                unit = gram[:, u % 2, 0:UQ * 2 * G].rearrange("f (q n) -> f q n", n=2 * G)
                for quad in (2 * e, 2 * e + 1):
                    for j in range(QUADS):
                        g = quad % 2 * G + CHUNKS * j
                        last = copy(pairs[Q * j:Q * (j + 1), t % 2, :, Q * quad + u * UQ:Q * quad + (u + 1) * UQ],
                                    unit[Q * quad:Q * (quad + 1), :, g:g + CHUNKS].rearrange("f q c -> f c q"))
                last.then_inc(unit_moved[e], 1)

        @block.scalar
        def _(act):
            def relu_h1(t):
                act.wait_ge(vec_landed, 16)
                act.wait_ge(h1_done[0], t + 1)
                for n in range(2):
                    last = act.activation(h1[:, n, :], h1_ps[n], ACT.Relu, bias=b1[:, n:n + 1])
                last.then_inc(h1_relued[0], 1)

            def relu_h2(t):
                act.wait_ge(h2_done[0], t + 1)
                act.activation(h2[:, 0, :], h2_ps[0], ACT.Relu, bias=b2[:, 0:1]).then_inc(h2_relued[0], 1)

            def convert_ids(j):
                act.wait_ge(wide_landed[j], 16)
                if j >= 2:
                    act.wait_ge(onehot_ready, VC * (j - 1))
                act.copy(ids16[:, j % 2, :], ids_wide[:, j % 2, :]).then_inc(ids16_ready, 1)

            def high(j):
                if j >= TABLES:
                    act.wait_ge(found, j - TABLES + 1)
                for h, cs in enumerate(HALVES):
                    act.wait_ge(table_landed[j][h], 32)
                    act.copy(parts[:, j % TABLES, 0, cs], table[:, j % TABLES, cs]).then_inc(high_ready, 1)

            def middle(j):
                for h, cs in enumerate(HALVES):
                    act.wait_ge(residue_ready, 2 * j + h + 1)
                    act.copy(parts[:, j % TABLES, 1, cs], table[:, j % TABLES, cs]).then_inc(middle_ready, 1)

            def copy_found(j):
                act.wait_ge(found, j + 1)
                act.copy(cols[:, :, :, j].rearrange("d t b -> d (t b)"), found_ps[j % 2]).then_inc(found_copied, 1)

            def stage(s, k):
                if k == 0:
                    if s > 0:
                        relu_h2(s - 1)
                    move_units(act, act.copy, s, 0, 0, 2)
                if k == 1:
                    move_units(act, act.copy, s, 0, 2, 4)
                if k == 4:
                    relu_h1(s)

            convert_ids(0)
            high(0)
            middle(0)
            convert_ids(1)
            high(1)
            for j in range(RESIDENT):
                if j > 0:
                    copy_found(j - 1)
                if j == 1:
                    copy_dense(act, act.copy)
                for k in beside_lookup(j):
                    if bank(0, k) == 0:
                        copy_group(act, act.copy, 0, k)
                if j + 2 < RESIDENT:
                    convert_ids(j + 2)
                    high(j + 2)
                if j + 1 < RESIDENT:
                    middle(j + 1)
            copy_found(RESIDENT - 1)
            for k in BEFORE_STAGES:
                if bank(1, k) == 0:
                    copy_group(act, act.copy, 1, k)
            for s in range(TILES):
                for k in range(STAGES):
                    stage(s, k)
                    for g in beside_stage(s, k):
                        if bank(s + 1, g) == 0:
                            copy_group(act, act.copy, s + 1, g)
            relu_h2(LAST)

        @block.vector
        def _(dve):
            def relu_h1(t):
                dve.wait_ge(vec_landed, 16)
                dve.wait_ge(h1_done[1], t + 1)
                for n in range(2, C1):
                    last = dve.tensor_scalar(h1[:, n, :], h1_ps[n], b1[:, n:n + 1], 0.0, ALU.add, ALU.max)
                last.then_inc(h1_relued[1], 1)

            def relu_h2(t):
                dve.wait_ge(h2_done[1], t + 1)
                dve.tensor_scalar(h2[:, 1, :], h2_ps[1], b2[:, 1:2], 0.0, ALU.add, ALU.max).then_inc(h2_relued[1], 1)

            def copy_y(t):
                dve.wait_ge(y_done, t + 1)
                dve.tensor_copy(y_tiles[:, t, :, :],
                                y_ps.rearrange("o (k q) -> o k q", k=QUADS)).then_inc(y_copied, 1)

            def one_hot(j, cs):
                dve.wait_ge(ids16_ready, j + 1)
                if j >= 2:
                    dve.wait_ge(found, j - 1)
                for c in range(cs.start, cs.stop):
                    dve.tensor_scalar(onehot[:, j % 2, c, :], ids16[0:VP, j % 2, :], row_number[:, c:c + 1],
                                      None, ALU.is_equal).then_inc(onehot_ready, 1)

            def residue(j, h):
                dve.wait_ge(high_ready, 2 * j + h + 1)
                half = table[:, j % TABLES, HALVES[h]]
                dve.tensor_tensor(half, half, parts[:, j % TABLES, 0, HALVES[h]],
                                  ALU.subtract).then_inc(residue_ready, 1)

            def low(j, h):
                dve.wait_ge(middle_ready, 2 * j + h + 1)
                dve.tensor_tensor(parts[:, j % TABLES, 2, HALVES[h]], table[:, j % TABLES, HALVES[h]],
                                  parts[:, j % TABLES, 1, HALVES[h]], ALU.subtract).then_inc(low_ready, 1)

            def stage(s, k):
                if k == 0:
                    move_units(dve, dve.tensor_copy, s, 1, 0, 2)
                if k == 1:
                    move_units(dve, dve.tensor_copy, s, 1, 2, 4)
                if k == 2 and s > 0:
                    relu_h2(s - 1)
                    copy_y(s - 1)
                if k == 6:
                    relu_h1(s)

            dve.memset(cols[:, 0, :, F:SLOTS], 0.0)
            dve.memset(cols[:, 1, :, F:SLOTS], 0.0)
            dve.wait_ge(row_index_ready, 1)
            dve.tensor_copy(row_number[:], row_index[:]).then_inc(row_number_ready, 1)
            dve.wait_ge(row_number_ready, 1)
            one_hot(0, HALVES[0])
            residue(0, 0)
            one_hot(0, HALVES[1])
            residue(0, 1)
            low(0, 0)
            low(0, 1)
            for j in range(RESIDENT):
                for k in beside_lookup(j):
                    if bank(0, k) == 1:
                        copy_group(dve, dve.tensor_copy, 0, k)
                if j + 1 < RESIDENT:
                    residue(j + 1, 0)
                    residue(j + 1, 1)
                    one_hot(j + 1, slice(0, VC))
                    low(j + 1, 0)
                    low(j + 1, 1)
            for t in range(2, TILES):
                last = dve.memset(cols[:, t, :, F:SLOTS], 0.0)
            last.then_inc(cols_zeroed, 1)
            dve.wait_ge(w1d_landed, 16)
            dve.tensor_tensor(w1ds[:], w1d[:, 0, :], w1d[:, 1, :], ALU.add).then_inc(w1d_summed, 1)
            for k in BEFORE_STAGES:
                if bank(1, k) == 1:
                    copy_group(dve, dve.tensor_copy, 1, k)
            for s in range(TILES):
                for k in range(STAGES):
                    stage(s, k)
                    for g in beside_stage(s, k):
                        if bank(s + 1, g) == 1:
                            copy_group(dve, dve.tensor_copy, s + 1, g)
            relu_h2(LAST)
            copy_y(LAST)


def kernel(**inputs):
    import numpy as np
    import concourse.bacc as bacc
    from concourse.bass_utils import run_bass_kernel_spmd

    a = {k: np.ascontiguousarray(v) for k, v in inputs.items()}
    dense, ids = a["r_dense_features"], a["ids"]
    tables = [a[f"tbl_{n}"] for n in range(ids.shape[1])]
    w1, w2, w3 = a["W_top1"], a["W_top2"], a["W_top3"]
    D, F, N1 = dense.shape[1], len(tables) + 1, w1.shape[1]

    small_rows = min(len(t) for t in tables)
    small = [n for n, t in enumerate(tables) if len(t) == small_rows][:RESIDENT]
    order = small + [n for n in range(len(tables)) if n not in small]
    slot = {n: s + (s >= len(small)) for s, n in enumerate(order)}
    slot_of = [len(small)] + [slot[n] for n in range(len(tables))]

    w1_dense = np.ascontiguousarray(np.stack([w1[:D], w1[-D:]], axis=1))
    w1_pairs = np.zeros((P, CHUNKS, N1), w1.dtype)
    row = D
    for f in range(F):
        for g in range(f + 1, F):
            first, second = sorted((slot_of[f], slot_of[g]))
            w1_pairs[SLOTS * (second // CHUNKS) + first, second % CHUNKS] = w1[row]
            row += 1
    arrays = {
        "dense": dense, "ids": ids[:, order],
        "small_ids": ids[:, small].reshape(P, -1, len(small)).transpose(2, 1, 0).reshape(len(small), -1),
        **{f"table{s}": tables[n] for s, n in enumerate(order)},
        "w1_dense": w1_dense, "w1_pairs": w1_pairs,
        "w2": np.ascontiguousarray(w2.reshape(N1 // P, P, -1).transpose(1, 0, 2)),
        "vectors": np.concatenate([v.reshape(-1, P).T for v in (a["b_top1"], a["b_top2"], w3)], axis=1),
    }
    nc = bacc.Bacc("TRN2", target_bir_lowering=False, num_devices=1)
    ap = {k: nc.dram_tensor(k, v.shape, mybir.dt.from_np(v.dtype), kind="ExternalInput").ap()
          for k, v in arrays.items()}
    out = nc.dram_tensor("out", (dense.shape[0], 1), F32, kind="ExternalOutput").ap()
    dlrm_tower(nc, ap["dense"], ap["ids"], ap["small_ids"], [ap[f"table{s}"] for s in range(len(small))],
               [ap[f"table{s}"] for s in range(len(small), len(order))],
               ap["w1_dense"], ap["w1_pairs"], ap["w2"], ap["vectors"], out)
    arrays = {k: np.ascontiguousarray(v) for k, v in arrays.items()}
    return run_bass_kernel_spmd(nc, [arrays], core_ids=[0]).results[0]["out"]
```
